# Optimizing a Trainium2 kernel written in Bass

```python
import numpy as np
import jax
import jax.numpy as jnp

def _softmax(x, axis=-1):
    return jax.nn.softmax(x, axis=axis)

def _gelu(x):
    return jax.nn.gelu(x, approximate=True)

def _silu(x):
    return jax.nn.silu(x)

def _sigmoid(x):
    return jax.nn.sigmoid(x)

def _layernorm(x, axis=-1, eps=1e-05):
    m = jnp.mean(x, axis=axis, keepdims=True)
    v = jnp.var(x, axis=axis, keepdims=True)
    return (x - m) / jnp.sqrt(v + eps)

def _scatter_add(tgt, idx, src, axis=0):
    return tgt.at[idx].add(src)

def _segment_sum(src, seg, n):
    return jax.ops.segment_sum(src, seg, n)
kernel_name = 'mk_xattn_ffn_d1_seqx_r2_1e09b0'

def setup_inputs(seed: int=0):
    np.random.seed(seed)
    _w = jnp.asarray

    def _rec_inputs():
        import jax
        import jax.numpy as jnp
        _rk = jax.random.key(seed)
        x = -0.0005207 + 1.001 * jax.random.normal(jax.random.fold_in(_rk, 1), (32, 512, 512), jnp.float32)
        _lenS = 512 - jax.random.randint(jax.random.fold_in(_rk, 7), (32,), 0, max(1, 512 // 4) + 1, jnp.int32)
        _lenS2 = 512 - jax.random.randint(jax.random.fold_in(_rk, 8), (32,), 0, max(1, 512 // 4) + 1, jnp.int32)
        _ctx_1024P = jax.random.normal(jax.random.fold_in(_rk, 11), (32, 16, 512), jnp.float32)
        _ctx_1024c = jax.random.dirichlet(jax.random.fold_in(_rk, 511), 0.3 * jnp.ones((16,), jnp.float32), (32, 512))
        _ctx_1024t = jnp.einsum('bsk,bkd->bsd', _ctx_1024c, _ctx_1024P)
        _ctx_1024t = _ctx_1024t * jax.lax.rsqrt(jnp.mean(jnp.square(_ctx_1024t)) + 1e-12) * 0.953939
        ctx_1024 = -0.000514642 + 1.00011 * (_ctx_1024t + 0.3 * jax.random.normal(jax.random.fold_in(_rk, 611), (32, 512, 512), jnp.float32))
        return (x, ctx_1024)
    x, ctx_1024 = _rec_inputs()

    def _L0_xattn_setup():
        import jax, jax.numpy as jnp
        import numpy as np
        B, S, E, NH = (1, 1024, 512, 8)
        DH = E // NH
        EPS = 1e-06
        LN_EPS = 1e-05
        key = jax.random.key(seed)
        ks = jax.random.split(key, 8)
        q = jax.random.normal(ks[0], (B, S, E), dtype=jnp.float32)
        k = jax.random.normal(ks[1], (B, S, E), dtype=jnp.float32)
        v = jax.random.normal(ks[2], (B, S, E), dtype=jnp.float32)
        scale = 1.0 / np.sqrt(3 * E)
        igate_w = jax.random.normal(ks[3], (NH, 3 * E), dtype=jnp.float32) * scale
        igate_b = jax.random.normal(ks[4], (NH,), dtype=jnp.float32) * 0.1
        fgate_w = jax.random.normal(ks[5], (NH, 3 * E), dtype=jnp.float32) * scale
        fgate_b = jnp.linspace(3.0, 6.0, NH, dtype=jnp.float32)
        out_w = 1.0 + 0.1 * jax.random.normal(ks[6], (E,), dtype=jnp.float32)
        return {'q': q, 'k': k, 'v': v, 'igate_w': igate_w, 'igate_b': igate_b, 'fgate_w': fgate_w, 'fgate_b': fgate_b, 'out_w': out_w}
    _L0_xattn_all = _L0_xattn_setup()
    _L0_xattn_in = {k: v for k, v in _L0_xattn_all.items() if k in ('igate_w', 'igate_b', 'fgate_w', 'fgate_b', 'out_w')}
    del _L0_xattn_all

    def _L0_ffn_setup():
        import jax, jax.numpy as jnp
        import numpy as np
        S, B, D, H, DH = (2048, 8, 512, 16, 64)

        def _forward(x, Wg, Wq, bq, Wkv, bkv, Wo, bo, ln_g, ln_b):
            s_len, bsz, d_model = x.shape
            n_head, _, d_head = Wq.shape
            cap = s_len // n_head
            scale = 1.0 / d_head ** 0.5
            h = jnp.transpose(x, (1, 0, 2))
            t = h
            probs = jax.nn.softmax(h @ Wg, axis=-1)
            scores = jnp.transpose(probs, (0, 2, 1))
            _, idx = jax.lax.top_k(scores, cap)
            idx = jnp.sort(idx, axis=-1)
            hg = jnp.take_along_axis(h[:, None, :, :], idx[..., None], axis=2)
            hg = jnp.transpose(hg, (1, 0, 2, 3))
            q = jnp.einsum('hbcd,hde->hbce', hg, Wq) + bq[:, None, None, :]
            kv = jnp.einsum('hbcd,hde->hbce', hg, Wkv) + bkv[:, None, None, :]
            k, v = jnp.split(kv, 2, axis=-1)
            att = jnp.einsum('hbid,hbjd->hbij', q, k) * scale
            p = jax.nn.softmax(att, axis=1)
            av = jnp.einsum('hbij,hbjd->hbid', p, v)
            ao = jnp.einsum('hbid,hde->hbie', av, Wo) + bo
            tok = jnp.transpose(idx, (1, 0, 2))
            b_ids = jnp.arange(bsz)[None, :, None]
            outs = jnp.zeros_like(t).at[b_ids, tok].add(ao)
            y = t + outs
            mu = jnp.mean(y, axis=-1, keepdims=True)
            var = jnp.var(y, axis=-1, keepdims=True)
            yn = (y - mu) * jax.lax.rsqrt(var + 1e-05) * ln_g + ln_b
            return jnp.transpose(yn, (1, 0, 2))
        key = jax.random.key(seed)
        ks = jax.random.split(key, 6)
        s = 0.02
        return {'x': jax.random.normal(ks[0], (S, B, D), jnp.float32), 'attn_mask': jnp.zeros((S, S), jnp.bool_), 'Wg': jax.random.normal(ks[1], (D, H), jnp.float32) * s, 'Wq': jax.random.normal(ks[2], (H, D, DH), jnp.float32) * s, 'bq': jnp.zeros((H, DH), jnp.float32), 'Wkv': jax.random.normal(ks[3], (H, D, 2 * DH), jnp.float32) * s, 'bkv': jnp.zeros((H, 2 * DH), jnp.float32), 'Wo': jax.random.normal(ks[4], (H, DH, D), jnp.float32) * s, 'bo': jnp.zeros((D,), jnp.float32), 'ln_g': jnp.ones((D,), jnp.float32), 'ln_b': jnp.zeros((D,), jnp.float32)}
    _L0_ffn_all = _L0_ffn_setup()
    _L0_ffn_in = {k: v for k, v in _L0_ffn_all.items() if k in ('attn_mask', 'Wg', 'Wq', 'bq', 'Wkv', 'bkv', 'Wo', 'bo', 'ln_g', 'ln_b')}
    del _L0_ffn_all
    return {'x': x, 'ctx_1024': ctx_1024, 'L0_xattn_igate_w': _L0_xattn_in['igate_w'], 'L0_xattn_igate_b': _L0_xattn_in['igate_b'], 'L0_xattn_fgate_w': _L0_xattn_in['fgate_w'], 'L0_xattn_fgate_b': _L0_xattn_in['fgate_b'], 'L0_xattn_out_w': _L0_xattn_in['out_w'], 'L0_ffn_attn_mask': _L0_ffn_in['attn_mask'], 'L0_ffn_Wg': _L0_ffn_in['Wg'], 'L0_ffn_Wq': _L0_ffn_in['Wq'], 'L0_ffn_bq': _L0_ffn_in['bq'], 'L0_ffn_Wkv': _L0_ffn_in['Wkv'], 'L0_ffn_bkv': _L0_ffn_in['bkv'], 'L0_ffn_Wo': _L0_ffn_in['Wo'], 'L0_ffn_bo': _L0_ffn_in['bo'], 'L0_ffn_ln_g': _L0_ffn_in['ln_g'], 'L0_ffn_ln_b': _L0_ffn_in['ln_b']}

def reference(x, ctx_1024, L0_xattn_igate_w, L0_xattn_igate_b, L0_xattn_fgate_w, L0_xattn_fgate_b, L0_xattn_out_w, L0_ffn_attn_mask, L0_ffn_Wg, L0_ffn_Wq, L0_ffn_bq, L0_ffn_Wkv, L0_ffn_bkv, L0_ffn_Wo, L0_ffn_bo, L0_ffn_ln_g, L0_ffn_ln_b):
    import jax
    import jax.numpy as jnp

    def _L0_xattn_ref(q, k, v, igate_w, igate_b, fgate_w, fgate_b, out_w):
        import jax, jax.numpy as jnp
        import numpy as np
        B, S, E, NH = (1, 1024, 512, 8)
        DH = E // NH
        EPS = 1e-06
        LN_EPS = 1e-05
        Bq, Sq, Eq = q.shape
        nh = igate_b.shape[0]
        dh = Eq // nh
        gi = jnp.concatenate([q, k, v], axis=-1)
        ig = (gi @ igate_w.T + igate_b).transpose(0, 2, 1)
        fg = (gi @ fgate_w.T + fgate_b).transpose(0, 2, 1)
        qh = q.reshape(Bq, Sq, nh, dh).transpose(0, 2, 1, 3)
        kh = k.reshape(Bq, Sq, nh, dh).transpose(0, 2, 1, 3)
        vh = v.reshape(Bq, Sq, nh, dh).transpose(0, 2, 1, 3)
        log_f = jax.nn.log_sigmoid(fg)
        cs = jnp.cumsum(log_f, axis=-1)
        diff = cs[..., :, None] - cs[..., None, :]
        mask = jnp.tril(jnp.ones((Sq, Sq), dtype=bool))
        log_fg_mat = jnp.where(mask, diff, -jnp.inf)
        log_D = log_fg_mat + ig[..., None, :]
        max_log_D = jnp.max(log_D, axis=-1, keepdims=True)
        D = jnp.exp(log_D - max_log_D)
        qk = jnp.einsum('bhsd,bhtd->bhst', qh, kh) / jnp.sqrt(jnp.float32(dh))
        C = qk * D
        normalizer = jnp.maximum(jnp.abs(C.sum(-1, keepdims=True)), jnp.exp(-max_log_D))
        h = jnp.einsum('bhst,bhtd->bhsd', C / (normalizer + EPS), vh)
        mean = h.mean(-1, keepdims=True)
        var = ((h - mean) ** 2).mean(-1, keepdims=True)
        hn = (h - mean) / jnp.sqrt(var + LN_EPS)
        hn = hn * out_w.reshape(nh, dh)[None, :, None, :]
        return hn.transpose(0, 2, 1, 3).reshape(Bq, Sq, Eq)

    def _L0_ffn_ref(x, attn_mask, Wg, Wq, bq, Wkv, bkv, Wo, bo, ln_g, ln_b):
        import jax, jax.numpy as jnp
        import numpy as np
        S, B, D, H, DH = (2048, 8, 512, 16, 64)

        def _forward(x, Wg, Wq, bq, Wkv, bkv, Wo, bo, ln_g, ln_b):
            s_len, bsz, d_model = x.shape
            n_head, _, d_head = Wq.shape
            cap = s_len // n_head
            scale = 1.0 / d_head ** 0.5
            h = jnp.transpose(x, (1, 0, 2))
            t = h
            probs = jax.nn.softmax(h @ Wg, axis=-1)
            scores = jnp.transpose(probs, (0, 2, 1))
            _, idx = jax.lax.top_k(scores, cap)
            idx = jnp.sort(idx, axis=-1)
            hg = jnp.take_along_axis(h[:, None, :, :], idx[..., None], axis=2)
            hg = jnp.transpose(hg, (1, 0, 2, 3))
            q = jnp.einsum('hbcd,hde->hbce', hg, Wq) + bq[:, None, None, :]
            kv = jnp.einsum('hbcd,hde->hbce', hg, Wkv) + bkv[:, None, None, :]
            k, v = jnp.split(kv, 2, axis=-1)
            att = jnp.einsum('hbid,hbjd->hbij', q, k) * scale
            p = jax.nn.softmax(att, axis=1)
            av = jnp.einsum('hbij,hbjd->hbid', p, v)
            ao = jnp.einsum('hbid,hde->hbie', av, Wo) + bo
            tok = jnp.transpose(idx, (1, 0, 2))
            b_ids = jnp.arange(bsz)[None, :, None]
            outs = jnp.zeros_like(t).at[b_ids, tok].add(ao)
            y = t + outs
            mu = jnp.mean(y, axis=-1, keepdims=True)
            var = jnp.var(y, axis=-1, keepdims=True)
            yn = (y - mu) * jax.lax.rsqrt(var + 1e-05) * ln_g + ln_b
            return jnp.transpose(yn, (1, 0, 2))
        return _forward(x, Wg, Wq, bq, Wkv, bkv, Wo, bo, ln_g, ln_b)
    x = x + _L0_xattn_ref(_layernorm(x, axis=-1), ctx_1024, ctx_1024, L0_xattn_igate_w, L0_xattn_igate_b, L0_xattn_fgate_w, L0_xattn_fgate_b, L0_xattn_out_w)
    x = x + _L0_ffn_ref(_layernorm(x, axis=-1), L0_ffn_attn_mask, L0_ffn_Wg, L0_ffn_Wq, L0_ffn_bq, L0_ffn_Wkv, L0_ffn_bkv, L0_ffn_Wo, L0_ffn_bo, L0_ffn_ln_g, L0_ffn_ln_b)
    return x

_drawn_inputs = setup_inputs


def setup_inputs(seed=0):
    import zlib

    import numpy as np

    out = dict(_drawn_inputs(seed))
    spreads = {'L0_ffn_bq': (0.0, 2.0),
     'L0_ffn_bkv': (0.0, 2.0),
     'L0_ffn_bo': (0.0, 0.1),
     'L0_ffn_ln_g': (1.0, 0.2),
     'L0_ffn_ln_b': (0.0, 0.1)}
    factors = {'L0_xattn_igate_b': 64.0, 'L0_ffn_Wq': 8.0, 'L0_ffn_Wkv': 8.0, 'L0_ffn_Wo': 8.0}
    for name, (base, spread) in spreads.items():
        noise = np.random.default_rng([zlib.crc32(name.encode()), seed]).standard_normal(out[name].shape)
        drawn = base * np.exp(spread * noise) if base else spread * noise
        out[name] = jnp.asarray(drawn.astype(out[name].dtype))
    for name, factor in factors.items():
        out[name] = (out[name] * factor).astype(out[name].dtype)
    return out
```

```python
from contextlib import ExitStack

import concourse.bass as bass
from concourse import mybir

ALU = mybir.AluOpType
ACT = mybir.ActivationFunctionType
AX = mybir.AxisListType
F32 = mybir.dt.float32
BF16 = mybir.dt.bfloat16

P = 128
MASKED = -1.0e30
LOWEST = -3.0e38
LN_EPS = 1e-5
DEN_EPS = 1e-6


class Batch:

    def __init__(self, pair, rest):
        self.pair, self.rest, self.parity = pair, rest, rest % 2
        self.number = pair * 2 + rest
        self.half = pair + rest // 2

    def __add__(self, n):
        return Batch(self.pair, self.rest + n)


class Signal:

    def __init__(self, sem, per, unit=1):
        self.sem, self.per, self.unit = sem, per, unit

    def at(self, batch, k):
        return batch.number * (self.per * self.unit) + k * self.unit


def wait(eng, signal, batch, k):
    value = signal.at(batch, k)
    if not (isinstance(value, int) and value <= 0):
        eng.wait_ge(signal.sem, value)


def hold(eng, carrier):
    eng.sem_inc(carrier, 1)


def walk(eng, nb, iteration, ahead=1):
    def one(pair, rest, full=False):
        got = []
        for d in (-1, 0, 1, 2):
            n = rest + d
            got.append(Batch(pair, n) if full or 0 <= n < nb else None)
        iteration(*got)

    first = 2
    for it in range(-ahead, first):
        one(0, it)
    pairs = (nb - ahead - first) // 2
    if pairs:
        with eng.Fori(0, pairs) as j:
            for r in (first, first + 1):
                one(j, r, True)
    for it in range(first + 2 * pairs, nb + 1):
        one(0, it)


def lagged(prev, cur, v):
    return (cur, v) if v >= 0 else (prev, v + 4)


def recurrence_stage(nc, scope, nb, args, x1_dram, keep):
    x, ctx, consts, gate_w, gate_b, out_w, wg = args
    probs_all, stat_all = keep
    S, E = x.shape[1:]
    NC = S // P
    KC = E // P
    NH = 8
    DH = E // NH
    V = DH + 1
    NE = probs_all.shape[2]
    NG = 2 * NH
    GC = NG + NH

    def sb(name, shape, dt=F32):
        return scope.enter_context(nc.sbuf_tensor("rec_" + name, shape, dt))

    def psum(name, shape, dt=F32):
        return scope.enter_context(nc.psum_tensor("rec_" + name, shape, dt))

    def signal(name, per, unit=1):
        return Signal(scope.enter_context(nc.semaphore("rec_" + name)), per, unit)

    xr = sb("x_ring", [P, 4 * NC, E])
    cin = [sb(f"ctx{p}", [P, NC, E]) for p in range(2)]
    xh = sb("x_hat", [P, NC, E])
    qt = [sb(f"q_t{p}", [P, KC, S]) for p in range(2)]
    kt = [sb(f"k_t{p}", [P, KC, S]) for p in range(2)]
    v1 = [sb(f"v_one{p}", [P, NC, NH, V]) for p in range(2)]
    kw = sb("k_weighted", [P, NC - 1, NH, DH])
    dmat = [sb(f"d{i}", [P, 4 * P]) for i in range(2)]
    cmat = [sb(f"c{i}", [P, 4 * P]) for i in range(2)]
    inter = sb("inter", [P, 4, V])
    num = [sb(f"num{i}", [P, NH, V]) for i in range(2)]
    sq = sb("squares", [P, NH, DH])
    hn = [sb(f"hn{i}", [P, NH, DH]) for i in range(2)]
    state = sb("state", [P, 4, V])
    decay = sb("decay", [P, NC, 4])
    decayed = sb("decayed", [P, 4, V])
    yn = sb("y", [P, NC, E])
    yt = sb("y_t", [P, KC, NC, P])
    ident = sb("ident", [P, P])
    triu = sb("triu", [P, P])
    ones = sb("ones", [P, P])
    lastrow = sb("lastrow", [P, P])
    cb = sb("consts_bf", [P, 5 + 16, P], BF16)
    gw_in = sb("gate_w_in", [P, 3, KC, NG])
    gq = sb("gate_q", [P, KC, P])
    gk = sb("gate_k", [P, KC, P])
    gb4 = sb("gate_bias", [P, NC, P])
    w8 = sb("out_w8", [P, E])
    wr = sb("router_w", [P, KC, P])
    mhalf = sb("minus_half", [P, NH])
    gates = sb("gates", [P, NC, GC])
    absf = sb("abs_f", [P, NC, NH])
    lnf = sb("ln_f", [P, NC, NH])
    logf = sb("log_f", [P, NC, NH])
    cums = sb("cums", [P, NC, NH])
    gm = sb("gm", [P, 2, NC, NH])
    rest1 = sb("rest1", [P, 2, NC, NH])
    grow = sb("g_rows", [NH, S])
    mrow = sb("m_rows", [NH, S])
    mcol = sb("m_cols", [P, NC, NH])
    mend = sb("m_end", [P, NC, NH])
    exarg = sb("ex_arg", [P, 4, NC, NH])
    ex = [sb(f"ex{p}", [P, 4, NC, NH]) for p in range(2)]
    rin = sb("rows_in", [P, NC, 2, 4, NH], BF16)
    rows = [sb(f"rows{p}", [P, S], BF16) for p in range(2)]
    xstat = sb("x_stat", [P, NC, 6])
    xagg = sb("x_agg", [P, NC, 2])
    xve = sb("x_ve", [P, NC])
    xrn = sb("x_rn", [P, NC, 2])
    ystat = sb("y_stat", [P, NC, 6])
    yagg = sb("y_agg", [P, NC, 2])
    yve = sb("y_ve", [P, NC])
    yrn = [sb(f"y_rn{p}", [P, NC, 2]) for p in range(2)]
    den = [sb(f"den{i}", [P, NH]) for i in range(2)]
    ssum = [sb(f"ssum{i}", [P, NH]) for i in range(2)]
    harg = [sb(f"harg{i}", [P, NH]) for i in range(2)]
    hrs = [sb(f"hrs{i}", [P, NH]) for i in range(2)]
    logit = sb("logit", [P, NC, NE])
    lmax = sb("lmax", [P, NC])
    lexp = sb("lexp", [P, NC, NE])
    lsum = sb("lsum", [P, NC])
    lrec = sb("lrec", [P, NC])

    l_ps = [psum(f"l_ps{i}", [P, 4 * P]) for i in range(2)]
    s_ps = psum("s_ps", [P, 4 * P])
    o1_ps = psum("o1_ps", [P, 4 * P])
    o2_ps = psum("o2_ps", [P, 4 * P])
    u_ps = psum("u_ps", [P, 4 * P])
    tp_ps = psum("tp_ps", [P, 4 * P])
    sm_ps = psum("sm_ps", [P, 4 * P])

    x_in = [[signal(f"x_in{p}{c}", 1, 16) for c in range(NC)] for p in range(2)]
    c_in = [[signal(f"c_in{p}{c}", 1, 16) for c in range(NC)] for p in range(2)]
    x1_st = [[signal(f"x1_st{p}{c}", 1, 16) for c in range(NC)] for p in range(2)]
    const_in = signal("const_in", 1)
    setup = signal("setup", 1)
    ones_set = signal("ones_set", 1)
    x_var = signal("x_var", NC)
    x_tmp = signal("x_tmp", 4)
    x_link = signal("x_link", NC)
    y_link = signal("y_link", NC)
    x_rs = signal("x_rs", NC)
    x_hat = signal("x_hat_done", NC)
    a_tp = signal("a_tp", 2 * NC)
    a_ev = signal("a_ev", 2 * NC)
    sm_full = signal("sm_full", 6)
    sm_read = signal("sm_read", 6)
    a_link = signal("a_link", 4)
    absd = signal("absd", 1)
    splus_t = signal("splus_t", 1)
    splus = signal("splus", 1)
    logfd = signal("logfd", 1)
    g_done = signal("g_done", 1)
    m_done = signal("m_done", 1)
    rin_done = signal("rin_done", 1)
    exarg_done = signal("exarg_done", 1)
    ex_done = signal("ex_done", 1)
    v1_done = signal("v1_done", NC)
    kw_done = signal("kw_done", NC - 1)
    l_full = signal("l_full", 8)
    d_done = signal("d_done", 8)
    s_full = signal("s_full", 8)
    c_done = signal("c_done", 8)
    o1_full = signal("o1_full", 8)
    o2_full = signal("o2_full", 6)
    u_full = signal("u_full", 6)
    t_done = signal("t_done", 6)
    num_done = signal("num_done", 8)
    st_done = signal("st_done", 6)
    std_done = signal("std_done", 2)
    dec_done = signal("dec_done", 1)
    den_link = signal("den_link", 5 * NC)
    sq_done = signal("sq_done", NC)
    harg_done = signal("harg_done", NC)
    hrs_done = signal("hrs_done", NC)
    hn_done = signal("hn_done", NC)
    hw_done = signal("hw_done", NC)
    x1_done = signal("x1_done", NC)
    y_var = signal("y_var", NC)
    y_tmp = signal("y_tmp", 2 * NC)
    y_rs = signal("y_rs", NC)
    y_done = signal("y_done", NC)
    r_tp = signal("r_tp", NC)
    r_ev = signal("r_ev", NC)
    rt_full = signal("rt_full", NC)
    rt_read = signal("rt_read", 1)
    rt_link = signal("rt_link", 3)
    lsub_done = signal("lsub_done", 1)
    lexp_done = signal("lexp_done", 1)

    carrier = {e: signal("carrier_" + e, 1).sem for e in ("sp", "pool", "pe", "act", "dve")}
    NLOADS, NSETUP = 10, 9
    RT0 = 2 * P

    CTX, XHAT = 0, 4
    YT = {9: 0, 11: 1, 13: 2, 14: 3}
    RT = {12: 0, 13: 1, 14: 2, 15: 3}
    SMALL = {8: 1, 10: 2, 11: 3, 13: 4, 14: 5, 15: 6}
    TILES = {**{CTX + c: ("ctx", c) for c in range(NC)}, **{XHAT + c: ("x_hat", c) for c in range(NC)}}

    def ring(batch, c):
        slot = (batch.number % 4) * NC + c
        return xr[:, slot, :] if isinstance(slot, int) else xr[:, bass.ds(slot, 1), :].rearrange("p a e -> p (a e)")

    def dram_tile(t, batch, c):
        n = batch.number
        rowsl = slice(c * P, (c + 1) * P)
        return t[n, rowsl, :] if isinstance(n, int) else t[bass.ds(n, 1), rowsl, :].rearrange("a p e -> (a p) e")

    block = scope.enter_context(nc.Block())

    @block.sync
    def _(sp):
        for dst, src in ((ident, consts[0]), (triu, consts[1]), (ones, consts[2]), (lastrow, consts[3])):
            sp.dma_start(dst[:], src).then_inc(const_in.sem, 16)
        sp.dma_start(gw_in[:], gate_w).then_inc(const_in.sem, 16)
        sp.dma_start(gb4[:], gate_b).then_inc(const_in.sem, 16)
        sp.dma_start(w8[:], out_w).then_inc(const_in.sem, 16)
        sp.dma_start(wr[:], wg).then_inc(const_in.sem, 16)
        sp.dma_start(kt[0][:].rearrange("p k s -> p (k s)"), consts[4:20].rearrange("n p f -> p n f")
                     ).then_inc(const_in.sem, 16)
        sp.dma_start(kt[1][:, 0:2, :].rearrange("p k s -> p (k s)")[:, 0:5 * P],
                     consts[20:25].rearrange("n p f -> p n f")).then_inc(const_in.sem, 16)

        def load_x(batch, c):
            old = batch + -4
            p = batch.parity
            wait(sp, y_done, old, c + 1)
            hold(sp, carrier["sp"])
            before = batch + -2
            if not isinstance(batch.number, int) or before.number >= 0:
                wait(sp, x_var, before, c + 1)
                hold(sp, carrier["sp"])
            if not isinstance(batch.number, int) or old.number >= 0:
                sp.wait_ge(x1_st[p][c].sem, (old.half + 1) * 16)
            hold(sp, carrier["sp"])
            sp.dma_start(ring(batch, c), dram_tile(x, batch, c)).then_inc(x_in[p][c].sem, 16)

        def load_ctx(batch, c):
            p = batch.parity
            old = batch + -2
            if c < NC - 1:
                wait(sp, kw_done, old, c + 1)
                hold(sp, carrier["sp"])
            if not isinstance(batch.number, int) or old.number >= 0:
                wait(sp, v1_done, old, c + 1)
                hold(sp, carrier["sp"])
                wait(sp, a_tp, old, c + 1)
            hold(sp, carrier["sp"])
            sp.dma_start(cin[p][:, c, :], dram_tile(ctx, batch, c)).then_inc(c_in[p][c].sem, 16)

        def store(batch, c):
            wait(sp, x1_done, batch, c + 1)
            hold(sp, carrier["sp"])
            sp.dma_start(dram_tile(x1_dram, batch, c), ring(batch, c)).then_inc(x1_st[batch.parity][c].sem, 16)

        def iteration(prev, cur, nxt, after):
            if after is not None:
                for c in range(NC):
                    load_x(after, c)
            for c in range(NC):
                cc = (0, 1, 3, 2)[c]
                b, t = (prev, c + 2) if c < 2 else (cur, c - 2)
                if b is not None:
                    store(b, t)
                if after is not None:
                    load_ctx(after, cc)

        walk(sp, nb, iteration, ahead=2)
        for p in range(2):
            for c in range(NC):
                sp.wait_ge(x1_st[p][c].sem, 16 * (nb // 2))

    @block.gpsimd
    def _(pool):
        for p in range(2):
            nc.gpsimd.memset(v1[p][:], 1.0)
            nc.gpsimd.memset(rows[p][:], 0.0)
        nc.gpsimd.memset(rin[:], 0.0)
        nc.gpsimd.memset(exarg[:], 0.0)
        nc.gpsimd.memset(mhalf[:], -0.5).then_inc(ones_set.sem, 1)
        pool.wait_ge(ones_set.sem, 1)
        pool.wait_ge(setup.sem, NSETUP)

        def rsqrt(batch, k, var, tmp, done, tiles, agg, ve, rn):
            lo, hi = tiles.start, tiles.stop
            wait(pool, var, batch, hi)
            hold(pool, carrier["pool"])
            nc.gpsimd.tensor_scalar(ve[:, lo:hi], agg[:, lo:hi, 1], LN_EPS, None, ALU.add).then_inc(tmp.sem, 1)
            wait(pool, tmp, batch, 2 * k - 1)
            nc.gpsimd.tensor_tensor(rn[:, lo:hi, 0], ve[:, lo:hi], mhalf[:, 0:hi - lo], ALU.pow).then_inc(tmp.sem, 1)
            wait(pool, tmp, batch, 2 * k)
            hold(pool, carrier["pool"])
            for c in range(lo, hi):
                nc.gpsimd.tensor_scalar(rn[:, c, 1:2], agg[:, c, 0:1], rn[:, c, 0:1], -1.0,
                                        ALU.mult, ALU.mult).then_inc(done.sem, 1)

        def values(batch, c):
            if c == 0:
                wait(pool, sm_read, batch, 1)
                wait(pool, o1_full, batch + -2, 8)
            mean = gates[:, c, NG:GC].unsqueeze(2).broadcast_to([P, NH, DH])
            nc.gpsimd.tensor_tensor(v1[batch.parity][:, c, :, 0:DH],
                                    cin[batch.parity][:, c, :].rearrange("p (h d) -> p h d", h=NH),
                                    mean, ALU.subtract).then_inc(v1_done.sem, 1)

        def iteration(prev, cur, nxt, after):
            for u in range(8):
                c, e = divmod(u, 2)
                if cur is not None and e == 0 and c < NC - 1:
                    if c == 0:
                        wait(pool, u_full, cur + -1, 6)
                    wait(pool, ex_done, cur, 1)
                    w = ex[cur.parity][:, 1, c, :].unsqueeze(2).broadcast_to([P, NH, DH])
                    nc.gpsimd.tensor_tensor(kw[:, c], cin[cur.parity][:, c, :].rearrange("p (h d) -> p h d", h=NH),
                                            w, ALU.mult).then_inc(kw_done.sem, 1)
                if nxt is not None and u in (1, 2):
                    rsqrt(nxt, u, x_var, x_tmp, x_rs, slice(2 * u - 2, 2 * u), xagg, xve, xrn)
                if e == 1:
                    b, t = lagged(prev, cur, (u - 3) // 2)
                    if b is not None:
                        wait(pool, harg_done, b, t + 1)
                        nc.gpsimd.tensor_tensor(hrs[t % 2][:], harg[t % 2][:], mhalf[:], ALU.pow
                                                ).then_inc(hrs_done.sem, 1)
                    b, t = lagged(prev, cur, (u - 5) // 2)
                    if b is not None:
                        rsqrt(b, t + 1, y_var, y_tmp, y_rs, slice(t, t + 1), yagg, yve, yrn[b.parity])
                if e == 0:
                    b, t = lagged(prev, cur, (u - 4) // 2)
                    if b is not None:
                        h = hn[t % 2][:].rearrange("p h d -> p (h d)")
                        wait(pool, hn_done, b, t + 1)
                        nc.gpsimd.tensor_tensor(h, h, w8[:], ALU.mult).then_inc(hw_done.sem, 1)
                        wait(pool, hw_done, b, t + 1)
                        nc.gpsimd.tensor_tensor(ring(b, t), ring(b, t), h, ALU.add).then_inc(x1_done.sem, 1)
                if cur is not None and e == 0 and 1 <= c < NC - 1:
                    wait(pool, st_done, cur, 2 * c)
                    wait(pool, dec_done, cur, 1)
                    dec = decay[:, c, :].unsqueeze(2).broadcast_to([P, 4, V])
                    nc.gpsimd.tensor_tensor(decayed[:], state[:], dec, ALU.mult).then_inc(std_done.sem, 1)
                if cur is not None and u in (1, 3):
                    values(cur, (u + 3) // 2)
                if nxt is not None and u in (6, 7):
                    values(nxt, u - 6)

        walk(pool, nb, iteration)

    @block.tensor
    def _(pe):
        pe.wait_ge(const_in.sem, 16 * NLOADS)
        pe.wait_ge(setup.sem, NSETUP)
        pe.wait_ge(ones_set.sem, 1)
        ident_bf, mask_bf = cb[:, 0, :], cb[:, 1:5, :]
        sel_g = cb[:, 5:13, :]
        sel_m = cb[:, 13:21, :]

        def begin_small(batch, k):
            b = batch
            if k > 1:
                wait(pe, sm_read, b, k - 1)
            else:
                wait(pe, sm_read, b + -1, 6)
            hold(pe, carrier["pe"])

        def transposes(src, c):
            for k in range(KC):
                mm = nc.tensor.transpose(tp_ps[:, k * P:(k + 1) * P], src[:, c, k * P:(k + 1) * P], ident[:])
            return mm

        def tile_gates(batch, n):
            c, ctx_part = n % NC, n < NC
            if n == 0:
                begin_small(batch, 1)
                wait(pe, rt_read, batch + -3, 1)
                hold(pe, carrier["pe"])
                nc.tensor.matmul(sm_ps[:, 0:NC * P], lastrow[:], gb4[:].rearrange("p c g -> p (c g)"),
                                 start=True, stop=False)
            wait(pe, a_ev, batch, n + 1)
            hold(pe, carrier["pe"])
            src, w = (kt, gk) if ctx_part else (qt, gq)
            for kc in range(KC):
                mm = nc.tensor.matmul(sm_ps[:, c * P:(c + 1) * P], src[batch.parity][:, kc, c * P:(c + 1) * P],
                                      w[:, kc, :], start=False, stop=(n == 2 * NC - 1 and kc == KC - 1))
            if n == 2 * NC - 1:
                mm.then_inc(sm_full.sem, 1)

        def small_group(nxt, k):
            if k == 2:
                wait(pe, logfd, nxt, 1)
                lf = logf[:].rearrange("p c h -> p (c h)")
                nc.tensor.matmul(sm_ps[:, 0:NC * NH], triu[:], lf, start=True, stop=False)
                for d in range(1, NC):
                    mm = nc.tensor.matmul(sm_ps[:, d * NH:NC * NH], ones[:], lf[:, 0:(NC - d) * NH],
                                          start=False, stop=(d == NC - 1))
            elif k == 3:
                wait(pe, g_done, nxt, 1)
                for c in range(NC):
                    mm = nc.tensor.transpose(sm_ps[0:NH, c * P:(c + 1) * P], gm[:, 0, c, :], ident[:])
            elif k == 4:
                wait(pe, m_done, nxt, 1)
                hold(pe, carrier["pe"])
                for c in range(NC):
                    mm = nc.tensor.transpose(sm_ps[:, c * NH:(c + 1) * NH], mrow[:, c * P:(c + 1) * P],
                                             ident[0:NH, 0:NH])
            elif k == 5:
                mm = nc.tensor.matmul(sm_ps[:, 0:NC * NH], lastrow[:], mcol[:].rearrange("p c h -> p (c h)"),
                                      start=True, stop=True)
            elif k == 6:
                wait(pe, rin_done, nxt, 1)
                hold(pe, carrier["pe"])
                o = sm_ps[0:64, 0:256].bitcast(BF16)
                for c in range(NC):
                    mm = nc.tensor.transpose(o[:, c * P:(c + 1) * P],
                                             rin[:, c].rearrange("p a b h -> p (a b h)"), ident_bf)
            mm.then_inc(sm_full.sem, 1)

        def router_logits(prev, c):
            wait(pe, r_ev, prev, c + 1)
            hold(pe, carrier["pe"])
            for k in range(KC):
                mm = nc.tensor.matmul(sm_ps[:, RT0 + c * NE:RT0 + c * NE + P], yt[:, k, c, :], wr[:, k, :],
                                      start=(k == 0), stop=(k == KC - 1))
            mm.then_inc(rt_full.sem, 1)

        def slot(s, prev, cur, nxt):
            if nxt is not None and s in TILES:
                kind, c = TILES[s]
                p = nxt.parity
                if s == 0:
                    wait(pe, r_ev, nxt + -3, NC)
                else:
                    wait(pe, a_ev, nxt, s)
                if kind == "x_hat":
                    wait(pe, x_hat, nxt, c + 1)
                    transposes(xh, c).then_inc(a_tp.sem, 1)
                else:
                    pe.wait_ge(c_in[p][c].sem, (nxt.half + 1) * 16)
                    transposes(cin[p], c).then_inc(a_tp.sem, 1)
            if nxt is not None and 0 <= s - CTX - 1 < 2 * NC:
                tile_gates(nxt, s - CTX - 1)
            if nxt is not None and SMALL.get(s, 0) > 1:
                begin_small(nxt, SMALL[s])
            if nxt is not None and RT.get(s) == 0:
                begin_small(nxt, SMALL[s - 1] + 1)
            if prev is not None and s in RT:
                router_logits(prev, RT[s])
            if nxt is not None and SMALL.get(s, 0) > 1:
                small_group(nxt, SMALL[s])
            if prev is not None and s in YT:
                c = YT[s]
                if c == 0:
                    if nxt is not None:
                        wait(pe, a_ev, nxt, 2 * NC)
                    else:
                        wait(pe, r_ev, prev + -1, NC)
                else:
                    wait(pe, r_ev, prev, c)
                wait(pe, y_done, prev, c + 1)
                transposes(yn, c).then_inc(r_tp.sem, 1)

        def log_d(cur, u):
            c, e = divmod(u, 2)
            p = cur.parity
            o = l_ps[u % 2]
            if u == 0:
                wait(pe, sm_read, cur, 6)
            wait(pe, d_done, cur, u - 1)
            nc.tensor.matmul(o[:], ident_bf, mask_bf.rearrange("p k s -> p (k s)"), start=True, stop=False)
            cols = rows[p][:, c * P:(c + 1) * P]
            nc.tensor.matmul(o[:], cols, sel_g[:, 4 * e:4 * e + 4, :].rearrange("p k s -> p (k s)"),
                             start=False, stop=False)
            for k in range(4):
                mm = nc.tensor.matmul(o[:, k * P:(k + 1) * P], sel_m[:, 4 * e + k, :], cols, start=False, stop=(k == 3))
            mm.then_inc(l_full.sem, 1)

        def scores(cur, u):
            c, e = divmod(u, 2)
            p, r, t = cur.parity, slice(DH * e, DH * (e + 1)), slice(c * P, (c + 1) * P)
            wait(pe, c_done, cur, u)
            for k in range(4):
                mm = nc.tensor.matmul(s_ps[:, k * P:(k + 1) * P], kt[p][r, k, t], qt[p][r, k, t], start=True, stop=True)
            mm.then_inc(s_full.sem, 1)

        def products(b, u):
            c, e = divmod(u, 2)
            p, r, t = b.parity, slice(DH * e, DH * (e + 1)), slice(c * P, (c + 1) * P)
            wait(pe, c_done, b, u + 1)
            wait(pe, num_done, b, u)
            if e == 0:
                wait(pe, v1_done, b, c + 1)
            for k in range(4):
                mm = nc.tensor.matmul(o1_ps[:, k * V:(k + 1) * V], cmat[u % 2][:, k * P:(k + 1) * P],
                                      v1[p][:, c, 2 * k + e, :], start=True, stop=True)
            mm.then_inc(o1_full.sem, 1)
            if c > 0:
                wait(pe, st_done, b, u - 1)
                wait(pe, t_done, b, u - 2)
                for k in range(4):
                    mm = nc.tensor.matmul(o2_ps[:, k * V:(k + 1) * V], qt[p][r, k, t], state[r, k, :],
                                          start=True, stop=True)
                mm.then_inc(o2_full.sem, 1)
            if c < NC - 1:
                if e == 0:
                    wait(pe, kw_done, b, c + 1)
                wait(pe, st_done, b, u)
                for k in range(4):
                    mm = nc.tensor.matmul(u_ps[r, k * V:(k + 1) * V], kw[:, c, 2 * k + e, :], v1[p][:, c, 2 * k + e, :],
                                          start=True, stop=True)
                mm.then_inc(u_full.sem, 1)

        def iteration(prev, cur, nxt, after):
            for u in range(8):
                if u == 0:
                    if prev is not None:
                        products(prev, 7)
                    slot(0, prev, cur, nxt)
                    if cur is not None:
                        log_d(cur, 0)
                        scores(cur, 0)
                else:
                    if cur is not None:
                        scores(cur, u)
                    slot(2 * u, prev, cur, nxt)
                    if cur is not None:
                        products(cur, u - 1)
                slot(2 * u + 1, prev, cur, nxt)
                if u < 7 and cur is not None:
                    log_d(cur, u + 1)

        walk(pe, nb, iteration)

    @block.scalar
    def _(act):
        act.wait_ge(setup.sem, NSETUP)

        def normalise(batch, c, rs, rn, src, dst, done):
            wait(act, rs, batch, c + 1)
            hold(act, carrier["act"])
            nc.scalar.activation(dst[:, c, :], src, ACT.Identity, bias=rn[:, c, 1:2], scale=rn[:, c, 0:1]
                                 ).then_inc(done.sem, 1)

        def slot(s, prev, cur, nxt):
            if nxt is not None and s in TILES:
                kind, c = TILES[s]
                dst = (qt if kind == "x_hat" else kt)[nxt.parity][:, :, c * P:(c + 1) * P]
                wait(act, a_tp, nxt, s + 1)
                nc.scalar.activation(dst, tp_ps[:].rearrange("p (k s) -> p k s", k=KC), ACT.Copy,
                                     scale=(DH ** -0.5 if kind == "x_hat" else 1.0)).then_inc(a_ev.sem, 1)
            if prev is not None and s in YT:
                c = YT[s]
                wait(act, rt_full, prev + -1, c + 1)
                wait(act, r_tp, prev, c + 1)
                nc.scalar.activation(yt[:, :, c, :], tp_ps[:].rearrange("p (k s) -> p k s", k=KC), ACT.Copy
                                     ).then_inc(r_ev.sem, 1)
            if nxt is not None and SMALL.get(s) == 1:
                wait(act, absd, nxt, 1)
                nc.scalar.activation(lnf[:], absf[:], ACT.Exp, scale=-1.0).then_inc(splus_t.sem, 1)
                wait(act, splus_t, nxt, 1)
                nc.scalar.activation(lnf[:], lnf[:], ACT.Ln, bias=1.0).then_inc(splus.sem, 1)
            if nxt is not None and s == 15:
                wait(act, exarg_done, nxt, 1)
                nc.scalar.activation(ex[nxt.parity][:], exarg[:], ACT.Exp).then_inc(ex_done.sem, 1)

        def iteration(prev, cur, nxt, after):
            for u in range(8):
                if u == 0:
                    slot(0, prev, cur, nxt)
                if cur is not None:
                    wait(act, l_full, cur, u + 1)
                    wait(act, c_done, cur, u - 1)
                    nc.scalar.activation(dmat[u % 2][:], l_ps[u % 2][:], ACT.Exp).then_inc(d_done.sem, 1)
                if u > 0:
                    slot(2 * u, prev, cur, nxt)
                slot(2 * u + 1, prev, cur, nxt)
                if nxt is not None and u in (1, 2):
                    for c in (2 * u - 2, 2 * u - 1):
                        wait(act, a_tp, nxt + -1, NC + c + 1)
                        normalise(nxt, c, x_rs, xrn, ring(nxt, c), xh, x_hat)
                if u % 2 == 1:
                    b, c = lagged(prev, cur, (u - 5) // 2)
                    if b is not None:
                        wait(act, r_tp, b + -1, c + 1)
                        normalise(b, c, y_rs, yrn[b.parity], ring(b, c), yn, y_done)
                if u % 2 == 0:
                    b, c = lagged(prev, cur, (u - 2) // 2)
                    if b is not None:
                        wait(act, num_done, b, 2 * c + 2)
                        wait(act, harg_done, b, c)
                        nc.scalar.activation(sq[:], num[c % 2][:, :, 0:DH], ACT.Square).then_inc(sq_done.sem, 1)
                if u == 7 and prev is not None:
                    wait(act, lsub_done, prev, 1)
                    nc.scalar.activation(lexp[:], logit[:], ACT.Exp).then_inc(lexp_done.sem, 1)

        walk(act, nb, iteration)

    @block.vector
    def _(dve):
        vec = nc.vector
        dve.wait_ge(const_in.sem, 16 * NLOADS)
        vec.memset(gq[:], 0.0).then_inc(setup.sem, 1)
        vec.memset(gk[:, :, GC:P], 0.0)
        vec.tensor_tensor(gk[:, :, 0:NG], gw_in[:, 1], gw_in[:, 2], ALU.add).then_inc(setup.sem, 1)
        vec.tensor_copy(gk[:, :, NG:GC], kt[1][:, 1, 0:KC * NH].rearrange("p (k h) -> p k h", k=KC)
                        ).then_inc(setup.sem, 1)
        dve.wait_ge(setup.sem, 1)
        vec.tensor_scalar(gq[:, :, 0:NG], gw_in[:, 0], DH ** 0.5, None, ALU.mult).then_inc(setup.sem, 1)
        vec.tensor_scalar(w8[:], w8[:], DH ** 0.5, None, ALU.mult).then_inc(setup.sem, 1)
        vec.tensor_copy(cb[:, 5:21, :].rearrange("p n f -> p (n f)"), kt[0][:].rearrange("p k s -> p (k s)")
                        ).then_inc(setup.sem, 1)
        vec.tensor_copy(cb[:, 0:1, :].rearrange("p n f -> p (n f)"), ident[:]).then_inc(setup.sem, 1)
        vec.tensor_copy(cb[:, 1:5, :], kt[1][:, 0, 0:P].unsqueeze(1).broadcast_to([P, 4, P])).then_inc(setup.sem, 1)
        vec.memset(state[:], 0.0).then_inc(setup.sem, 1)
        dve.wait_ge(setup.sem, NSETUP)
        dve.wait_ge(ones_set.sem, 1)

        def moments(batch, c, src, stat, agg, tmp, var):
            hold(dve, carrier["dve"])
            vec.bn_stats(stat[:, c, :], src).then_inc(tmp.sem, 1)
            wait(dve, tmp, batch, c + 1)
            hold(dve, carrier["dve"])
            vec.bn_aggr(agg[:, c, :], stat[:, c, :]).then_inc(var.sem, 1)

        def read_small(batch, k):
            wait(dve, sm_full, batch, k)

        def link(ins, sig, batch, k):
            ins.then_inc(sig.sem, 1)
            wait(dve, sig, batch, k)

        flat = "p c h -> p (c h)"

        def gates_step(s, nxt, prev):
            if nxt is not None and s in SMALL:
                k = SMALL[s]
                read_small(nxt, k)
                if k == 1:
                    wait(dve, v1_done, nxt + -1, NC)
                    vec.tensor_copy(gates[:], sm_ps[:].rearrange("p (c g) -> p c g", c=NC)[:, :, 0:GC]
                                    ).then_inc(sm_read.sem, 1)
                    wait(dve, sm_read, nxt, 1)
                    f = gates[:, :, NH:NG]
                    vec.scalar_tensor_tensor(absf[:], f, -1.0, f, ALU.mult, ALU.max).then_inc(absd.sem, 1)
                elif k == 2:
                    vec.tensor_copy(cums[:].rearrange(flat), sm_ps[:, 0:NC * NH]).then_inc(sm_read.sem, 1)
                    wait(dve, sm_read, nxt, 2)
                    vec.tensor_tensor(gm[:, 0], gates[:, :, 0:NH], cums[:], ALU.subtract).then_inc(g_done.sem, 1)
                elif k == 3:
                    vec.tensor_copy(grow[:], sm_ps[0:NH, :]).then_inc(sm_read.sem, 1)
                    wait(dve, sm_read, nxt, 3)
                    vec.tensor_tensor_scan(mrow[:], grow[:], grow[:], LOWEST, ALU.max, ALU.max
                                           ).then_inc(m_done.sem, 1)
                elif k == 4:
                    vec.tensor_copy(mcol[:].rearrange(flat), sm_ps[:, 0:NC * NH]).then_inc(sm_read.sem, 1)
                    wait(dve, sm_read, nxt, 4)
                    link(vec.tensor_scalar(gm[:, 1], mcol[:], -1.0, None, ALU.mult), a_link, nxt, 1)
                    link(vec.tensor_copy(rin[:, :, :, 0, :], gm[:].rearrange("p a c h -> p c a h")), a_link, nxt, 2)
                    link(vec.tensor_tensor(rest1[:], gm[:], rin[:, :, :, 0, :].rearrange("p c a h -> p a c h"),
                                           ALU.subtract), a_link, nxt, 3)
                    link(vec.tensor_copy(rin[:, :, :, 1, :], rest1[:].rearrange("p a c h -> p c a h")), a_link, nxt, 4)
                    vec.tensor_tensor(rin[:, :, :, 2, :], rest1[:].rearrange("p a c h -> p c a h"),
                                      rin[:, :, :, 1, :], ALU.subtract).then_inc(rin_done.sem, 1)
                elif k == 5:
                    vec.tensor_copy(mend[:].rearrange(flat), sm_ps[:, 0:NC * NH]).then_inc(sm_read.sem, 1)
                    wait(dve, sm_read, nxt, 5)
                    wait(dve, ex_done, nxt + -1, 1)
                    vec.tensor_tensor(exarg[:, 0, 1:NC], mend[:, 0:NC - 1], mcol[:, 1:NC], ALU.subtract)
                    vec.tensor_tensor(exarg[:, 1], gm[:, 0], mend[:], ALU.subtract)
                    vec.scalar_tensor_tensor(exarg[:, 2].rearrange(flat), cums[:].rearrange(flat), -1.0,
                                             mcol[:].rearrange(flat), ALU.mult, ALU.subtract)
                    vec.tensor_tensor(exarg[:, 3, 1:NC], mend[:, 0:NC - 1], mend[:, 1:NC], ALU.subtract
                                      ).then_inc(exarg_done.sem, 1)
                elif k == 6:
                    vec.tensor_copy(rows[nxt.parity][0:64, :], sm_ps[0:64, 0:256].bitcast(BF16)
                                    ).then_inc(sm_read.sem, 1)

        def read_router(prev):
            wait(dve, lexp_done, prev + -1, 1)
            wait(dve, rt_full, prev, NC)
            vec.tensor_copy(logit[:].rearrange(flat), sm_ps[:, RT0:RT0 + NC * NE]).then_inc(rt_read.sem, 1)
            wait(dve, rt_read, prev, 1)
            link(vec.tensor_reduce(lmax[:], logit[:], AX.X, ALU.max), rt_link, prev, 1)
            vec.tensor_tensor(logit[:], logit[:], lmax[:].unsqueeze(2).broadcast_to([P, NC, NE]), ALU.subtract
                              ).then_inc(lsub_done.sem, 1)
            n = prev.number
            wait(dve, y_rs, prev, NC)
            vec.tensor_copy(stat_all[:, :, :, n] if isinstance(n, int) else
                            stat_all[:, :, :, bass.ds(n, 1)].rearrange("p j c b -> p j (c b)"),
                            yrn[prev.parity][:].rearrange("p c j -> p j c"))
            wait(dve, lexp_done, prev, 1)
            link(vec.tensor_reduce(lsum[:], lexp[:], AX.X, ALU.add), rt_link, prev, 2)
            link(vec.reciprocal(lrec[:], lsum[:]), rt_link, prev, 3)
            vec.tensor_tensor(probs_all[:, :, :, n] if isinstance(n, int) else
                              probs_all[:, :, :, bass.ds(n, 1)].rearrange("p c h b -> p c (h b)"),
                              lexp[:], lrec[:].unsqueeze(2).broadcast_to([P, NC, NE]), ALU.mult)

        def log_forget(nxt):
            wait(dve, splus, nxt, 1)
            vec.scalar_tensor_tensor(logf[:], gates[:, :, NH:NG], 0.0, lnf[:], ALU.min, ALU.subtract
                                     ).then_inc(logfd.sem, 1)

        def weigh(cur, u):
            wait(dve, s_full, cur, u + 1)
            wait(dve, d_done, cur, u + 1)
            wait(dve, o1_full, cur, u - 1)
            vec.tensor_tensor(cmat[u % 2][:], s_ps[:], dmat[u % 2][:], ALU.mult).then_inc(c_done.sem, 1)

        def gather_products(b, u):
            c, e = divmod(u, 2)
            r = slice(DH * e, DH * (e + 1))
            n = num[c % 2][:].rearrange("p (k e) d -> p e k d", e=2)[:, e]
            o1 = o1_ps[:, 0:4 * V].rearrange("p (k d) -> p k d", k=4)
            if c > 0:
                wait(dve, o2_full, b, u - 1)
                em = ex[b.parity][:, 0, c, e::2].unsqueeze(2).broadcast_to([P, 4, V])
                vec.tensor_tensor(inter[:], o2_ps[:, 0:4 * V].rearrange("p (k d) -> p k d", k=4), em, ALU.mult
                                  ).then_inc(t_done.sem, 1)
                wait(dve, o1_full, b, u + 1)
                wait(dve, t_done, b, u - 1)
                vec.tensor_tensor(n, o1, inter[:], ALU.add).then_inc(num_done.sem, 1)
            else:
                wait(dve, o1_full, b, u + 1)
                vec.tensor_copy(n, o1).then_inc(num_done.sem, 1)
            if c < NC - 1:
                up = u_ps[r, 0:4 * V].rearrange("p (k d) -> p k d", k=4)
                wait(dve, u_full, b, u + 1)
                if c == 0:
                    wait(dve, o2_full, b + -1, 6)
                    vec.tensor_copy(state[r], up).then_inc(st_done.sem, 1)
                else:
                    wait(dve, std_done, b, c)
                    vec.tensor_tensor(state[r], decayed[r], up, ALU.add).then_inc(st_done.sem, 1)

        def denominators(b, c):
            i = c % 2
            n1 = num[i][:, :, DH]
            wait(dve, num_done, b, 2 * c + 2)
            link(vec.scalar_tensor_tensor(den[i][:], n1, -1.0, n1, ALU.mult, ALU.max), den_link, b, 5 * c + 1)
            wait(dve, ex_done, b, 1)
            link(vec.tensor_tensor(den[i][:], den[i][:], ex[b.parity][:, 2, c, :], ALU.max), den_link, b, 5 * c + 2)
            link(vec.tensor_scalar(den[i][:], den[i][:], DEN_EPS, None, ALU.add), den_link, b, 5 * c + 3)
            link(vec.tensor_tensor(den[i][:], den[i][:], den[i][:], ALU.mult), den_link, b, 5 * c + 4)

        def variances(b, c):
            i = c % 2
            wait(dve, sq_done, b, c + 1)
            link(vec.tensor_reduce(ssum[i][:], sq[:], AX.X, ALU.add), den_link, b, 5 * c + 5)
            vec.scalar_tensor_tensor(harg[i][:], den[i][:], DH * LN_EPS, ssum[i][:], ALU.mult, ALU.add
                                     ).then_inc(harg_done.sem, 1)

        def head_norm(b, c):
            i = c % 2
            wait(dve, hrs_done, b, c + 1)
            wait(dve, x1_done, b, c - 1)
            vec.tensor_tensor(hn[i][:], num[i][:, :, 0:DH], hrs[i][:].unsqueeze(2).broadcast_to([P, NH, DH]),
                              ALU.mult).then_inc(hn_done.sem, 1)

        def iteration(prev, cur, nxt, after):
            for u in range(8):
                if u == 0 and prev is not None:
                    gather_products(prev, 7)
                if cur is not None:
                    weigh(cur, u)
                if u == 0 and cur is not None:
                    wait(dve, ex_done, cur, 1)
                    for e in range(2):
                        r = slice(DH * e, DH * (e + 1))
                        ins = vec.tensor_copy(decay[r], ex[cur.parity][r, 3, :, e::2])
                    ins.then_inc(dec_done.sem, 1)
                if u % 2 == 1:
                    b, c = lagged(prev, cur, (u - 3) // 2)
                    if b is not None:
                        variances(b, c)
                gates_step(2 * u, nxt, prev)
                if u > 0 and cur is not None:
                    gather_products(cur, u - 1)
                if nxt is not None and u == 4:
                    log_forget(nxt)
                gates_step(2 * u + 1, nxt, prev)
                if u % 2 == 0:
                    b, c = lagged(prev, cur, (u - 2) // 2)
                    if b is not None:
                        denominators(b, c)
                    b, c = lagged(prev, cur, (u - 4) // 2)
                    if b is not None:
                        wait(dve, x1_done, b, c + 1)
                        wait(dve, y_done, b + -1, c + 1)
                        moments(b, c, ring(b, c), ystat, yagg, y_link, y_var)
                else:
                    b, c = lagged(prev, cur, (u - 3) // 2)
                    if b is not None:
                        head_norm(b, c)
                if nxt is not None and u < 2:
                    for c in (2 * u, 2 * u + 1):
                        dve.wait_ge(x_in[nxt.parity][c].sem, (nxt.half + 1) * 16)
                        wait(dve, x_hat, nxt + -1, c + 1)
                        moments(nxt, c, ring(nxt, c), xstat, xagg, x_link, x_var)
                if u == 7 and prev is not None:
                    read_router(prev)

        walk(dve, nb, iteration)



class Step:

    def __init__(self, number):
        self.number = number


class Credit(Signal):

    def __init__(self, sem, per, credit, unit=1):
        super().__init__(sem, per, unit)
        self.credit = credit

    def at(self, step, k):
        return super().at(step, k) + self.credit


class Shapes:
    def __init__(self, NB, S, E, NE, DH):
        self.NB, self.S, self.E, self.NE, self.DH = NB, S, E, NE, DH
        self.TOP = NB // NE
        self.PK = NE * self.TOP
        self.G = P // NB
        self.NC = S // P
        self.T = P // self.G
        self.KC = E // P
        assert self.PK == NB and self.TOP == 2 and self.T % 8 == 0


def routing_tables(nc, scope, z, keep, tables, consts):
    probs_all, stat_all = keep
    idxp, statp, tokid, ident = tables
    C2 = z.NC * z.NE

    def sb(name, shape, dt=F32):
        return scope.enter_context(nc.sbuf_tensor("top_" + name, shape, dt))

    def sem(name):
        return scope.enter_context(nc.semaphore("top_" + name))

    eq = sb("eq", [P, C2, z.NB])
    left = sb("left", [P, C2, z.NB])
    iotab = sb("iotab", [P, z.NB + 1])
    m1 = sb("m1", [P, C2])
    first = sb("first", [P, C2])
    second = sb("second", [P, C2])
    idx = sb("idx", [P, C2, 2])
    ip_ps = scope.enter_context(nc.psum_tensor("ip_ps", [P, 4 * P], F32))
    st_ps = scope.enter_context(nc.psum_tensor("st_ps", [P, 4 * P], F32))
    const_in, link_s, idx_done, tab_full = sem("const2_in"), sem("top_link"), sem("idx_done"), sem("tab_full")
    block = scope.enter_context(nc.Block())

    @block.sync
    def _(sp):
        sp.dma_start(ident[:], consts[0]).then_inc(const_in, 16)
        sp.dma_start(tokid[:], consts[25]).then_inc(const_in, 16)
        sp.dma_start(iotab[:], consts[26, :, 0:z.NB + 1]).then_inc(const_in, 16)

    @block.vector
    def _(dve):
        vec = nc.vector
        n = [0]

        def link(ins):
            n[0] += 1
            ins.then_inc(link_s, 1)
            dve.wait_ge(link_s, n[0])

        full = [P, C2, z.NB]
        probs = probs_all[:].rearrange("p c h b -> p (c h) b")
        iota = iotab[:, 0:z.NB].unsqueeze(1).broadcast_to(full)
        dve.wait_ge(const_in, 48)

        def top(src, index):
            link(vec.tensor_reduce(m1[:], src, AX.X, ALU.max))
            link(vec.tensor_tensor(eq[:], src, m1[:].unsqueeze(2).broadcast_to(full), ALU.is_equal))
            link(vec.tensor_tensor(eq[:], eq[:], iota, ALU.mult))
            link(vec.tensor_reduce(index[:], eq[:], AX.X, ALU.min))

        top(probs, first)
        link(vec.tensor_tensor(eq[:], iota, first[:].unsqueeze(2).broadcast_to(full), ALU.is_equal))
        link(vec.scalar_tensor_tensor(left[:].rearrange("p c b -> p (c b)"), eq[:].rearrange("p c b -> p (c b)"), -2.0,
                                      probs.rearrange("p c b -> p (c b)"), ALU.mult, ALU.add))
        top(left[:], second)
        vec.tensor_tensor(idx[:, :, 0], first[:], second[:], ALU.min)
        vec.tensor_tensor(idx[:, :, 1], first[:], second[:], ALU.max).then_inc(idx_done, 1)
        dve.wait_ge(tab_full, 1)
        vec.tensor_scalar(idxp[:], ip_ps[:, 0:z.NC * z.T], iotab[:, z.NB:z.NB + 1], None, ALU.add)
        vec.tensor_copy(statp[:].rearrange("p j n -> p (j n)"), st_ps[:, 0:2 * z.NC * z.T])

    @block.tensor
    def _(pe):
        pe.wait_ge(const_in, 48)
        pe.wait_ge(idx_done, 1)
        for c in range(z.NC):
            for g in range(z.G):
                o, rows, rhs = slice(c * z.T, (c + 1) * z.T), slice(g * z.NB, (g + 1) * z.NB), slice(g * z.T, (g + 1) * z.T)
                nc.tensor.matmul(ip_ps[rows, o], idx[:, c * z.NE:(c + 1) * z.NE, :].rearrange("p h i -> p (h i)"),
                                 ident[:, rhs], start=True, stop=True)
                for j in range(2):
                    oj = slice(j * z.NC * z.T + c * z.T, j * z.NC * z.T + (c + 1) * z.T)
                    mm = nc.tensor.matmul(st_ps[rows, oj], stat_all[:, j, c, :], ident[:, rhs], start=True, stop=True)
        mm.then_inc(tab_full, 1)


def attention_logits(nc, scope, z, x1_dram, wqkv, bqkv, tables, vall, att):
    idxp, statp, tokid, ident = tables
    W3 = 3 * z.DH
    DH = z.DH

    def sb(name, shape, dt=F32):
        return scope.enter_context(nc.sbuf_tensor("log_" + name, shape, dt))

    def psum(name):
        return scope.enter_context(nc.psum_tensor("log_" + name, [P, 4 * P], F32))

    def sem(name):
        return scope.enter_context(nc.semaphore("log_" + name))

    w = sb("wqkv", [P, z.NE, z.KC, W3])
    bias = sb("bqkv", [P, z.NE, W3])
    xq = [sb(f"x1_quad{i}", [P, 4, z.E]) for i in range(2)]
    y = [sb(f"y_tile{i}", [P, z.E]) for i in range(2)]
    p2 = [sb(f"hot{i}", [P, 4, P]) for i in range(2)]
    pt = [sb(f"hot_t{i}", [P, 4, P]) for i in range(2)]
    gt = sb("gathered_t", [P, z.KC, z.PK, P])
    qk = [sb(f"qk{i}", [P, 2, 2 * DH]) for i in range(2)]
    prod = [sb(f"prod{i}", [P, 4, 4, DH]) for i in range(2)]
    g_ps = [psum(f"g_ps{i}") for i in range(2)]
    h_ps = [psum(f"h_ps{i}") for i in range(2)]
    q_ps = [psum(f"q_ps{i}") for i in range(2)]

    NQ = z.T // 4
    w_in = sem("w_in")
    x_in = [Signal(sem(f"x1q_in{i}"), 1, 64) for i in range(2)]
    y_done = Credit(sem("y2_done"), 1, 8)
    hot_done = Credit(sem("hot_done"), 1, 2)
    ht_full = Credit(sem("ht_full"), 1, 2)
    pt_done = Credit(sem("pt_done"), 1, 2)
    g_full = Credit(sem("g_full"), 1, 8)
    g_out = [Credit(sem(f"g_out{i}"), 1, 2) for i in range(2)]
    q_full = Credit(sem("q_full"), z.NE, 2)
    q_out = Credit(sem("q_out"), z.NE, 2)
    prod_done = Credit(sem("prod_done"), z.NE, 8)
    att_done = Credit(sem("att_done"), z.NE // 4, 2)
    block = scope.enter_context(nc.Block())

    def quads(eng, c, body):
        with eng.Fori(0, NQ // 2) as j:
            for r in range(2):
                body(c * NQ + j * 2 + r, r, (j * 2 + r) * 4, c * (NQ // 2) + j)

    def copy_out(eng, m, half, t, which, c):
        wait(eng, g_full, Step(m), 1)
        wait(eng, q_full, Step(c), 0)
        src = g_ps[which][:].rearrange("p (k g h) -> p k g h", k=z.KC, g=z.G)
        dst = gt[:].rearrange("p k h (g t) -> p k g h t", g=z.G)[:, :, :, :, bass.ds(t, 1)].rearrange(
            "p k g h t -> p k g (h t)")
        if which == 0:
            ins = nc.scalar.activation(dst, src, ACT.Copy)
        else:
            ins = nc.vector.tensor_copy(dst, src)
        ins.then_inc(g_out[which].sem, 1)

    @block.sync
    def _(sp):
        sp.dma_start(w[:], wqkv).then_inc(w_in, 16)
        sp.dma_start(bias[:], bqkv).then_inc(w_in, 16)
        view = x1_dram.rearrange("s (c g t) e -> c g s (t e)", c=z.NC, g=z.G)
        with sp.Fori(0, z.NC) as c:
            def body(n, r, t0, half):
                sp.wait_ge(y_done.sem, n * 4 - 4 + 8)
                for g in range(z.G):
                    src = view[bass.ds(c, 1), g, :, bass.ds(t0 * z.E, 4 * z.E)].rearrange("a s f -> (a s) f")
                    sp.dma_start(xq[r][g * z.NB:(g + 1) * z.NB].rearrange("p t e -> p (t e)"), src
                                 ).then_inc(x_in[r].sem, 16)
            quads(sp, c, body)

    @block.scalar
    def _(act):
        act.sem_inc(y_done.sem, y_done.credit)
        act.sem_inc(g_out[0].sem, g_out[0].credit)
        with act.Fori(0, z.NC) as c:
            def body(n, r, t0, half):
                act.wait_ge(x_in[r].sem, half * 64 + 64)
                for i in range(4):
                    m, col = n * 4 + i, c * z.T + t0 + i
                    wait(act, g_full, Step(m), -1)
                    nc.scalar.activation(y[i % 2][:], xq[r][:, i, :], ACT.Identity,
                                         bias=statp[:, 1, bass.ds(col, 1)], scale=statp[:, 0, bass.ds(col, 1)]
                                         ).then_inc(y_done.sem, 1)
                    if i % 2 == 1:
                        copy_out(act, m - 1, n * 2 + i // 2, t0 + i - 1, 0, c)
            quads(act, c, body)

    @block.vector
    def _(dve):
        vec = nc.vector
        for s in (hot_done, pt_done, g_out[1], q_out, att_done):
            dve.sem_inc(s.sem, s.credit)
        dve.wait_ge(w_in, 32)
        with dve.Fori(0, z.NC) as c:
            def body(n, r, t0, half):
                wait(dve, ht_full, Step(n), -1)
                for i in range(4):
                    ins = vec.tensor_scalar(p2[r][:, i, :], tokid[:], idxp[:, bass.ds(c * z.T + t0 + i, 1)], None,
                                            ALU.is_equal)
                ins.then_inc(hot_done.sem, 1)
                wait(dve, ht_full, Step(n), 1)
                wait(dve, g_full, Step(n * 4), -4)
                vec.tensor_copy(pt[r][:].rearrange("p t f -> p (t f)"), h_ps[r][:]).then_inc(pt_done.sem, 1)
                for i in (1, 3):
                    copy_out(dve, n * 4 + i, n * 2 + i // 2, t0 + i, 1, c)
            quads(dve, c, body)
            ch = Step(c)

            def logits(hq):
                wait(dve, prod_done, ch, 4 * hq + 4)
                vec.tensor_reduce(att[:, bass.ds(c, 1), hq * 16:hq * 16 + 16].rearrange("p a k -> p (a k)"),
                                  prod[hq % 2][:].rearrange("p h k d -> p (h k) d"), AX.X, ALU.add
                                  ).then_inc(att_done.sem, 1)

            for h in range(z.NE):
                wait(dve, q_full, ch, h + 1)
                wait(dve, prod_done, ch, h - 1)
                src = q_ps[h % 2][:, 0:2 * W3].rearrange("p (i f) -> p i f", i=2)
                vec.tensor_tensor(vall[:, bass.ds(c, 1), h, :, :].rearrange("p a i d -> p (a i) d"),
                                  src[:, :, 2 * DH:], bias[:, h, 2 * DH:].unsqueeze(1).broadcast_to([P, 2, DH]), ALU.add)
                vec.tensor_tensor(qk[h % 2][:], src[:, :, 0:2 * DH],
                                  bias[:, h, 0:2 * DH].unsqueeze(1).broadcast_to([P, 2, 2 * DH]), ALU.add
                                  ).then_inc(q_out.sem, 1)
                if h % 4 == 1 and h > 4:
                    logits(h // 4 - 1)
            logits(z.NE // 4 - 1)

    @block.gpsimd
    def _(pool):
        pool.sem_inc(prod_done.sem, prod_done.credit)
        with pool.Fori(0, z.NC) as c:
            ch = Step(c)
            for h in range(z.NE):
                wait(pool, q_out, ch, h + 1)
                if h % 4 == 0:
                    wait(pool, att_done, ch, h // 4 - 1)
                q = qk[h % 2][:, :, 0:DH].unsqueeze(2).broadcast_to([P, 2, 2, DH])
                k = qk[h % 2][:, :, DH:2 * DH].unsqueeze(1).broadcast_to([P, 2, 2, DH])
                nc.gpsimd.tensor_tensor(prod[(h // 4) % 2][:, h % 4].rearrange("p (i j) d -> p i j d", i=2), q, k,
                                        ALU.mult).then_inc(prod_done.sem, 1)

    @block.tensor
    def _(pe):
        for s in (ht_full, g_full, q_full):
            pe.sem_inc(s.sem, s.credit)
        pe.wait_ge(w_in, 32)
        with pe.Fori(0, z.NC) as c:
            def body(n, r, t0, half):
                wait(pe, hot_done, Step(n), 1)
                wait(pe, pt_done, Step(n), -1)
                for i in range(4):
                    mm = nc.tensor.transpose(h_ps[r][:, i * P:(i + 1) * P], p2[r][:, i, :], ident[:])
                mm.then_inc(ht_full.sem, 1)
                wait(pe, pt_done, Step(n), 1)
                for i in range(4):
                    m = n * 4 + i
                    wait(pe, y_done, Step(m), 1)
                    wait(pe, g_out[i % 2], Step(n * 2 + i // 2), 0)
                    for k in range(z.KC):
                        mm = nc.tensor.matmul(g_ps[i % 2][:, k * P:(k + 1) * P], y[i % 2][:, k * P:(k + 1) * P],
                                              pt[r][:, i, :], start=True, stop=True)
                    mm.then_inc(g_full.sem, 1)
            quads(pe, c, body)
            wait(pe, g_out[0], Step(c * (z.T // 2)), z.T // 2)
            wait(pe, g_out[1], Step(c * (z.T // 2)), z.T // 2)
            ch = Step(c)
            for h in range(z.NE):
                wait(pe, q_out, ch, h - 1)
                for i in range(2):
                    for k in range(z.KC):
                        mm = nc.tensor.matmul(q_ps[h % 2][:, i * W3:(i + 1) * W3], gt[:, k, 2 * h + i, :], w[:, h, k, :],
                                              start=(k == 0), stop=(k == z.KC - 1))
                mm.then_inc(q_full.sem, 1)


def softmax_over_rows(nc, scope, z, att, tables):
    ident = tables[3]
    K = z.NE * 4
    mx = scope.enter_context(nc.sbuf_tensor("mx", [P, K], F32))
    mx1 = scope.enter_context(nc.sbuf_tensor("mx1", [K, 1], F32))
    mxb = scope.enter_context(nc.sbuf_tensor("mxb", [K, P], F32))
    ones = scope.enter_context(nc.sbuf_tensor("ones2", [P, P], F32))
    tot = scope.enter_context(nc.sbuf_tensor("tot", [P, K], F32))
    rec = scope.enter_context(nc.sbuf_tensor("rec", [P, K], F32))
    a_ps = scope.enter_context(nc.psum_tensor("a_ps", [P, 4 * P], F32))
    b_ps = scope.enter_context(nc.psum_tensor("b_ps", [P, 4 * P], F32))
    c_ps = scope.enter_context(nc.psum_tensor("c_ps", [P, 4 * P], F32))
    link_s = scope.enter_context(nc.semaphore("sm_link"))
    pe_s = scope.enter_context(nc.semaphore("sm_pe"))
    act_s = scope.enter_context(nc.semaphore("sm_act"))
    block = scope.enter_context(nc.Block())

    @block.vector
    def _(dve):
        vec = nc.vector
        n = [0]

        def link(ins):
            n[0] += 1
            ins.then_inc(link_s, 1)
            dve.wait_ge(link_s, n[0])

        flat = att[:].rearrange("p c k -> p (c k)")
        vec.memset(ones[:], 1.0)
        link(vec.tensor_reduce(mx[:], att[:].rearrange("p c k -> p k c"), AX.X, ALU.max))
        dve.wait_ge(pe_s, 1)
        link(vec.tensor_reduce(mx1[:], a_ps[0:K, 0:P], AX.X, ALU.max))
        link(vec.tensor_scalar(mxb[:], ones[0:K, :], mx1[:, 0:1], None, ALU.mult))
        dve.wait_ge(pe_s, 2)
        link(vec.tensor_tensor(att[:], att[:], b_ps[:, 0:K].unsqueeze(1).broadcast_to([P, z.NC, K]), ALU.subtract))
        dve.wait_ge(pe_s, 3)
        link(vec.tensor_reduce(tot[:], c_ps[:, 0:z.NC * K].rearrange("p (c k) -> p k c", c=z.NC), AX.X, ALU.add))
        link(vec.reciprocal(rec[:], tot[:]))
        link(vec.tensor_tensor(att[:], att[:], rec[:].unsqueeze(1).broadcast_to([P, z.NC, K]), ALU.mult))

    @block.scalar
    def _(act):
        act.wait_ge(link_s, 4)
        nc.scalar.activation(att[:], att[:], ACT.Exp, scale=z.DH ** -0.5).then_inc(act_s, 1)

    @block.tensor
    def _(pe):
        pe.wait_ge(link_s, 1)
        nc.tensor.transpose(a_ps[0:K, 0:P], mx[:], ident[:]).then_inc(pe_s, 1)
        pe.wait_ge(link_s, 3)
        nc.tensor.matmul(b_ps[:, 0:K], mxb[:], ident[0:K, 0:K], start=True, stop=True).then_inc(pe_s, 1)
        pe.wait_ge(act_s, 1)
        nc.tensor.matmul(c_ps[:, 0:z.NC * K], ones[:], att[:].rearrange("p c k -> p (c k)"),
                         start=True, stop=True).then_inc(pe_s, 1)


def output_stage(nc, scope, z, x1_dram, ao_dram, out, wo_in, vecs, tables, vall, att):
    idxp, statp, tokid, ident = tables
    DH, E = z.DH, z.E
    HP = z.NE // 2

    def sb(name, shape, dt=F32):
        return scope.enter_context(nc.sbuf_tensor("out_" + name, shape, dt))

    def psum(name):
        return scope.enter_context(nc.psum_tensor("out_" + name, [P, 4 * P], F32))

    def sem(name):
        return scope.enter_context(nc.semaphore("out_" + name))

    wo = sb("wo", [P, HP, E])
    bo = sb("bo", [P, E])
    lg = sb("ln_g", [P, E])
    lb = sb("ln_b", [P, E])
    mhalf = sb("mhalf2", [P, 1])
    t0b = sb("part0", [P, z.NE, DH])
    t1b = [sb(f"part1{i}", [P, z.NE, DH]) for i in range(2)]
    av = [sb(f"av{i}", [P, z.NE, DH]) for i in range(2)]
    avt = sb("av_t", [P, 2, HP, P])
    aob = [sb(f"ao{i}", [P, E]) for i in range(2)]
    aq = [sb(f"ao_quad{i}", [P, 4, E]) for i in range(2)]
    xq = [sb(f"x1_quad{i}", [P, 4, E]) for i in range(2)]
    oq = [sb(f"out_quad{i}", [P, 4, E]) for i in range(2)]
    y = [sb(f"y_tile{i}", [P, E]) for i in range(2)]
    xb = [sb(f"xb_tile{i}", [P, E]) for i in range(2)]
    zt = [sb(f"z_tile{i}", [P, E]) for i in range(2)]
    p2 = [sb(f"hot{i}", [P, P]) for i in range(2)]
    stat = [sb(f"zstat{i}", [P, 6]) for i in range(2)]
    agg = [sb(f"zagg{i}", [P, 2]) for i in range(2)]
    ve = [sb(f"zve{i}", [P, 1]) for i in range(2)]
    rs = [sb(f"zrs{i}", [P, 1]) for i in range(2)]
    t_ps = [psum(f"t_ps{i}") for i in range(2)]
    o_ps = [psum(f"o_ps{i}") for i in range(4)]
    z_ps = [psum(f"z_ps{i}") for i in range(2)]

    T, PK, NQ = z.T, z.PK, z.T // 4
    carrier = {e: sem("carrier_" + e) for e in ("pool", "dve")}
    w_in, ones_set = sem("wo_in"), sem("mh_set")
    av1_done = Signal(sem("av1_done"), 2)
    av_link = Signal(sem("av_link"), 2)
    av_done = Signal(sem("av_done"), 2)
    at_full = Signal(sem("at_full"), 4)
    at_out = Signal(sem("at_out"), 4)
    o_full = Signal(sem("o_full"), PK)
    o_out = Signal(sem("o_out"), PK)
    ao_st = [Signal(sem(f"ao_st{i}"), PK // 2, 16) for i in range(2)]
    a_in = [Signal(sem(f"a_in{i}"), NQ // 2, 16 * z.G) for i in range(2)]
    x_in = [Signal(sem(f"x2_in{i}"), NQ // 2, 16 * z.G) for i in range(2)]
    o_st = [Signal(sem(f"o_st{i}"), NQ // 2, 16 * z.G) for i in range(2)]
    y_done = Signal(sem("y3_done"), T)
    xb_done = Signal(sem("xb_done"), T)
    hot_done = Signal(sem("hot3_done"), T)
    z_full = Signal(sem("z_full"), T)
    z_done = Signal(sem("z_done"), T)
    z_link = Signal(sem("z_link"), T)
    z_var = Signal(sem("z_var"), T)
    z_tmp = Signal(sem("z_tmp"), T)
    z_rs = Signal(sem("z_rs"), T)
    zg_done = Signal(sem("zg_done"), T)
    out_done = Signal(sem("out_done"), T)
    block = scope.enter_context(nc.Block())

    def chunk_of(t, c):
        return t[c] if isinstance(c, int) else t[bass.ds(c, 1)].rearrange("a g s f -> (a g) s f")

    def schedule(eng, prepare, project, scatter):
        def turn(proj, scat):
            if proj is not None:
                prepare(proj)
            for s in range(z.NE):
                if proj is not None:
                    project(proj, s)
                if scat is not None:
                    for t in (2 * s, 2 * s + 1):
                        scatter(scat, t)

        turn(Step(0), None)
        turn(Step(1), Step(0))
        with eng.Fori(2, z.NC) as c:
            turn(Step(c), Step(c - 1))
        turn(None, Step(z.NC - 1))

    def nothing(*a):
        pass

    x_view = x1_dram.rearrange("s (c g t) e -> c g s (t e)", c=z.NC, g=z.G)
    o_view = out.rearrange("s (c g t) e -> c g s (t e)", c=z.NC, g=z.G)

    def att_of(c):
        a = att[:, c, :] if isinstance(c, int) else att[:, bass.ds(c, 1), :].rearrange("p a k -> p (a k)")
        return a.rearrange("p (h i j) -> p h i j", i=2, j=2)

    def v_of(c):
        return vall[:, c] if isinstance(c, int) else vall[:, bass.ds(c, 1)].rearrange("p a h j d -> p (a h) j d")

    @block.sync
    def _(sp):
        for dst, src in ((wo, wo_in), (bo, vecs[0]), (lg, vecs[1]), (lb, vecs[2])):
            sp.dma_start(dst[:], src).then_inc(w_in, 16)

        def project(ch, h):
            for i in range(2):
                k = 2 * h + i
                wait(sp, o_out, ch, k + 1)
                c = ch.number
                dst = ao_dram[c, :, k] if isinstance(c, int) else \
                    ao_dram[bass.ds(c, 1), :, k].rearrange("a g t e -> (a g) t e")
                sp.dma_start(dst, aob[i][:]).then_inc(ao_st[i].sem, 16)

        def scatter(ch, t):
            if t % 4 == 0:
                q, r = t // 4, (t // 4) % 2
                if q == 0:
                    for i in range(2):
                        wait(sp, ao_st[i], ch, PK // 2)
                wait(sp, z_full, ch, t - 4)
                wait(sp, out_done, ch, t - 4)
                a_view = ao_dram.rearrange("c g k t e -> c g k (t e)")
                for g in range(z.G):
                    sp.dma_start(aq[r][g * PK:(g + 1) * PK].rearrange("p t e -> p (t e)"),
                                 chunk_of(a_view, ch.number)[g, :, t * E:(t + 4) * E]).then_inc(a_in[r].sem, 16)
                    sp.dma_start(xq[r][g * z.NB:(g + 1) * z.NB].rearrange("p t e -> p (t e)"),
                                 chunk_of(x_view, ch.number)[g, :, t * E:(t + 4) * E]).then_inc(x_in[r].sem, 16)

        schedule(sp, nothing, project, scatter)

    @block.gpsimd
    def _(pool):
        nc.gpsimd.memset(mhalf[:], -0.5).then_inc(ones_set, 1)
        pool.wait_ge(ones_set, 1)
        pool.wait_ge(w_in, 64)

        def prepare(ch):
            c = ch.number
            for i in range(2):
                wait(pool, av_done, ch, i - 1)
                p = att_of(c)[:, :, i, 1]
                nc.gpsimd.tensor_tensor(t1b[i][:], v_of(c)[:, :, 1, :], p.unsqueeze(2).broadcast_to([P, z.NE, DH]),
                                        ALU.mult).then_inc(av1_done.sem, 1)

        def scatter(ch, t):
            b, r, i = t % 2, (t // 4) % 2, t % 4
            if i == 0:
                wait(pool, x_in[r], ch, t // 8 + 1)
            wait(pool, out_done, ch, t - 1)
            nc.gpsimd.tensor_tensor(xb[b][:], xq[r][:, i, :], lb[:], ALU.add).then_inc(xb_done.sem, 1)
            wait(pool, z_var, ch, t + 1)
            hold(pool, carrier["pool"])
            nc.gpsimd.tensor_scalar(ve[b][:], agg[b][:, 1:2], LN_EPS, None, ALU.add).then_inc(z_tmp.sem, 1)
            wait(pool, z_tmp, ch, t + 1)
            nc.gpsimd.tensor_tensor(rs[b][:], ve[b][:], mhalf[:], ALU.pow).then_inc(z_rs.sem, 1)

        schedule(pool, prepare, nothing, scatter)

    @block.scalar
    def _(act):
        def prepare(ch):
            for n in range(4):
                wait(act, at_full, ch, n + 1)
                if n == 0:
                    wait(act, o_full, ch, 0)
                nc.scalar.activation(avt[:, n // 2, 4 * (n % 2):4 * (n % 2) + 4, :].rearrange("p h b -> p (h b)"),
                                     t_ps[n % 2][:], ACT.Copy).then_inc(at_out.sem, 1)

        def scatter(ch, t):
            b, r, i = t % 2, (t // 4) % 2, t % 4
            if i == 0:
                wait(act, x_in[r], ch, t // 8 + 1)
            wait(act, z_done, ch, t - 1)
            c = ch.number
            cols = [statp[:, j, c * T + t:c * T + t + 1] if isinstance(c, int) else
                    statp[:, j, bass.ds(c * T + t, 1)] for j in range(2)]
            nc.scalar.activation(y[b][:], xq[r][:, i, :], ACT.Identity, bias=cols[1], scale=cols[0]
                                 ).then_inc(y_done.sem, 1)
            if i == 3:
                wait(act, out_done, ch, t + 1)
                for g in range(z.G):
                    act.dma_start(chunk_of(o_view, ch.number)[g, :, (t - 3) * E:(t + 1) * E],
                                  oq[r][g * z.NB:(g + 1) * z.NB].rearrange("p t e -> p (t e)")
                                  ).then_inc(o_st[r].sem, 16)

        schedule(act, prepare, nothing, scatter)
        for r in range(2):
            act.wait_ge(o_st[r].sem, z.NC * (NQ // 2) * 16 * z.G)

    @block.tensor
    def _(pe):
        pe.wait_ge(w_in, 64)

        def prepare(ch):
            for n in range(4):
                i = n // 2
                wait(pe, av_done, ch, i + 1)
                wait(pe, at_out, ch, n - 1)
                for m in range(4):
                    hp = 4 * (n % 2) + m
                    mm = nc.tensor.transpose(t_ps[n % 2][:, m * P:(m + 1) * P],
                                             av[i][:, 2 * hp:2 * hp + 2, :].rearrange("p h d -> p (h d)"), ident[:])
                mm.then_inc(at_full.sem, 1)

        def project(ch, h):
            r = slice(DH * (h % 2), DH * (h % 2 + 1))
            if h == 0:
                wait(pe, at_out, ch, 4)
            for i in range(2):
                k = 2 * h + i
                wait(pe, o_out, ch, k - 3)
                nc.tensor.matmul(o_ps[k % 4][:], avt[r, i, h // 2, :], wo[r, h // 2, :], start=True, stop=True
                                 ).then_inc(o_full.sem, 1)

        def scatter(ch, t):
            b, r, i = t % 2, (t // 4) % 2, t % 4
            if i == 0:
                wait(pe, a_in[r], ch, t // 8 + 1)
            wait(pe, hot_done, ch, t + 1)
            wait(pe, z_done, ch, t - 1)
            nc.tensor.matmul(z_ps[b][:], p2[b][:], aq[r][:, i, :], start=True, stop=True).then_inc(z_full.sem, 1)

        schedule(pe, prepare, project, scatter)

    @block.vector
    def _(dve):
        vec = nc.vector
        dve.wait_ge(w_in, 64)
        dve.wait_ge(ones_set, 1)

        def prepare(ch):
            c = ch.number
            for i in range(2):
                p = att_of(c)[:, :, i, 0]
                wait(dve, av_done, ch, i)
                vec.tensor_tensor(t0b[:], v_of(c)[:, :, 0, :], p.unsqueeze(2).broadcast_to([P, z.NE, DH]), ALU.mult
                                  ).then_inc(av_link.sem, 1)
                wait(dve, av_link, ch, i + 1)
                wait(dve, av1_done, ch, i + 1)
                wait(dve, at_full, ch, 2 * i - 2)
                vec.tensor_tensor(av[i][:], t0b[:], t1b[i][:], ALU.add).then_inc(av_done.sem, 1)

        def project(ch, h):
            for i in range(2):
                k = 2 * h + i
                wait(dve, o_full, ch, k + 1)
                if not (isinstance(ch.number, int) and ch.number == 0 and h == 0):
                    dve.wait_ge(ao_st[i].sem, ch.number * (PK * 8) + h * 16)
                vec.tensor_tensor(aob[i][:], o_ps[k % 4][:], bo[:], ALU.add).then_inc(o_out.sem, 1)

        def scatter(ch, t):
            b, r, i = t % 2, (t // 4) % 2, t % 4
            c = ch.number
            wait(dve, z_full, ch, t - 1)
            col = idxp[:, c * T + t:c * T + t + 1] if isinstance(c, int) else idxp[:, bass.ds(c * T + t, 1)]
            vec.tensor_scalar(p2[b][:], tokid[:], col, None, ALU.is_equal).then_inc(hot_done.sem, 1)
            wait(dve, y_done, ch, t + 1)
            wait(dve, z_full, ch, t + 1)
            vec.tensor_tensor(zt[b][:], y[b][:], z_ps[b][:], ALU.add).then_inc(z_done.sem, 1)
            wait(dve, z_done, ch, t + 1)
            vec.bn_stats(stat[b][:], zt[b][:]).then_inc(z_link.sem, 1)
            wait(dve, z_link, ch, t + 1)
            hold(dve, carrier["dve"])
            vec.bn_aggr(agg[b][:], stat[b][:]).then_inc(z_var.sem, 1)
            wait(dve, z_var, ch, t + 1)
            vec.scalar_tensor_tensor(zt[b][:], zt[b][:], agg[b][:, 0:1], lg[:], ALU.subtract, ALU.mult
                                     ).then_inc(zg_done.sem, 1)
            wait(dve, zg_done, ch, t + 1)
            wait(dve, xb_done, ch, t + 1)
            wait(dve, z_rs, ch, t + 1)
            if i == 0:
                wait(dve, o_st[r], ch, t // 8)
            vec.scalar_tensor_tensor(oq[r][:, i, :], zt[b][:], rs[b][:, 0:1], xb[b][:], ALU.mult, ALU.add
                                     ).then_inc(out_done.sem, 1)

        schedule(dve, prepare, project, scatter)


def program(nc, x, ctx, consts, gate_w, gate_b, out_w, wg, wqkv, bqkv, wo, vecs, out, x1_dram, ao_dram):
    NB, S, E = x.shape
    NE = wqkv.shape[1]
    z = Shapes(NB, S, E, NE, wqkv.shape[3] // 3)
    with ExitStack() as kept:
        def sb(scope, name, shape):
            return scope.enter_context(nc.sbuf_tensor(name, shape, F32))

        idxp = sb(kept, "idxp", [P, z.NC * z.T])
        statp = sb(kept, "statp", [P, 2, z.NC * z.T])
        tokid = sb(kept, "tokid", [P, P])
        ident = sb(kept, "ident2", [P, P])
        tables = (idxp, statp, tokid, ident)
        with ExitStack() as routed:
            keep = (sb(routed, "probs_all", [P, z.NC, NE, NB]), sb(routed, "stat_all", [P, 2, z.NC, NB]))
            with ExitStack() as scope:
                recurrence_stage(nc, scope, NB, (x, ctx, consts, gate_w, gate_b, out_w, wg), x1_dram, keep)
            with ExitStack() as scope:
                routing_tables(nc, scope, z, keep, tables, consts)
        vall = sb(kept, "v_all", [P, z.NC, NE, 2, z.DH])
        att = sb(kept, "att", [P, z.NC, NE * 4])
        with ExitStack() as scope:
            attention_logits(nc, scope, z, x1_dram, wqkv, bqkv, tables, vall, att)
        with ExitStack() as scope:
            softmax_over_rows(nc, scope, z, att, tables)
        with ExitStack() as scope:
            output_stage(nc, scope, z, x1_dram, ao_dram, out, wo, vecs, tables, vall, att)

def shape_constants():
    import numpy as np
    c = np.zeros((27, 128, 128), np.float32)
    c[0] = np.eye(128)
    c[1] = np.triu(np.ones((128, 128)))
    c[2] = 1.0
    c[3, 127, :] = 1.0
    for e in range(2):
        for k in range(4):
            h = 2 * k + e
            for part in range(3):
                c[4 + 4 * e + k, 8 * part + h, :] = 1.0
                c[12 + 4 * e + k, 32 + 8 * part + h, :] = 1.0
    c[20] = np.where(np.arange(128)[:, None] > np.arange(128)[None, :], MASKED, 0.0)
    for k in range(4):
        for e in range(128):
            c[24, e, 8 * k + 2 * k + e // 64] = 1.0 / 64
    c[25] = np.arange(128)
    c[26, :, 0:32] = np.arange(32) - 64.0
    c[26, :, 32] = np.arange(128) // 32 * 32 + 64.0
    return c


def gate_layout(igate_w, fgate_w):
    import numpy as np
    w = np.concatenate([igate_w, fgate_w], 0)
    return np.ascontiguousarray(w.reshape(16, 3, 4, 128).transpose(3, 1, 2, 0))


def gate_bias_layout(igate_b, fgate_b):
    import numpy as np
    b = np.concatenate([igate_b, fgate_b, np.zeros(128 - 16, igate_b.dtype)])
    return np.ascontiguousarray(np.broadcast_to(b, (128, 4, 128)))


def kernel(**inputs):
    import numpy as np
    import concourse.bacc as bacc
    from concourse.bass_utils import run_bass_kernel_spmd

    a = {k: np.asarray(v) for k, v in inputs.items()}
    rows = lambda v: np.ascontiguousarray(np.broadcast_to(v, (P,) + v.shape))
    wg, wq, wkv, wo = a["L0_ffn_Wg"], a["L0_ffn_Wq"], a["L0_ffn_Wkv"], a["L0_ffn_Wo"]
    E, NE = wg.shape
    DH = wq.shape[2]
    wqkv = np.concatenate([wq, wkv], 2).reshape(NE, E // P, P, 3 * DH).transpose(2, 0, 1, 3)
    arrays = {
        "x": a["x"], "ctx": a["ctx_1024"], "consts": shape_constants(),
        "gate_w": gate_layout(a["L0_xattn_igate_w"], a["L0_xattn_fgate_w"]),
        "gate_b": gate_bias_layout(a["L0_xattn_igate_b"], a["L0_xattn_fgate_b"]),
        "out_w": rows(a["L0_xattn_out_w"]), "wg": np.pad(wg, ((0, 0), (0, P - NE))).reshape(E // P, P, P).transpose(1, 0, 2),
        "wqkv": wqkv, "bqkv": rows(np.concatenate([a["L0_ffn_bq"], a["L0_ffn_bkv"]], 1)),
        "wo": wo.reshape(NE // 2, 2 * DH, E).transpose(1, 0, 2),
        "vecs": np.stack([rows(a["L0_ffn_bo"]), rows(a["L0_ffn_ln_g"]), rows(a["L0_ffn_ln_b"])]),
    }
    arrays = {k: np.ascontiguousarray(v) for k, v in arrays.items()}
    arrays = {"in_" + k: v for k, v in arrays.items()}
    nc = bacc.Bacc("TRN2", target_bir_lowering=False, num_devices=1)
    aps = [nc.dram_tensor(k, v.shape, F32, kind="ExternalInput").ap() for k, v in arrays.items()]
    shape = arrays["in_x"].shape
    out = nc.dram_tensor("out", shape, F32, kind="ExternalOutput").ap()
    x1_dram = nc.dram_tensor("x1_scratch", shape, F32, kind="Internal").ap()
    G, T = P // shape[0], shape[0]
    ao_dram = nc.dram_tensor("ao_scratch", (shape[1] // P, G, 2 * NE, T, E), F32, kind="Internal").ap()
    program(nc, *aps, out, x1_dram, ao_dram)
    return run_bass_kernel_spmd(nc, [arrays], core_ids=[0]).results[0]["out"]
```
